# Optimizing a Trainium2 kernel written in Bass

```python
import numpy as np
import jax
import jax.numpy as jnp

def _softmax(x, axis=-1):
    return jax.nn.softmax(x, axis=axis)

def _gelu(x):
    return jax.nn.gelu(x, approximate=True)

def _silu(x):
    return jax.nn.silu(x)

def _sigmoid(x):
    return jax.nn.sigmoid(x)

def _layernorm(x, axis=-1, eps=1e-05):
    m = jnp.mean(x, axis=axis, keepdims=True)
    v = jnp.var(x, axis=axis, keepdims=True)
    return (x - m) / jnp.sqrt(v + eps)

def _scatter_add(tgt, idx, src, axis=0):
    return tgt.at[idx].add(src)

def _segment_sum(src, seg, n):
    return jax.ops.segment_sum(src, seg, n)
kernel_name = 'mk_macaron_d1_jaxref_r8_4bf8b1'

def setup_inputs(seed: int=0):
    np.random.seed(seed)
    _w = jnp.asarray

    def _L0_attn_setup():
        import jax, jax.numpy as jnp
        import numpy as np
        B, T, D = (4, 256, 256)
        H = 16
        HD = D // H
        key = jax.random.key(seed)
        ks = jax.random.split(key, 10)
        s = 0.02
        return {'x': jax.random.normal(ks[0], (B, T, D), dtype=jnp.float32), 'Wq': jax.random.normal(ks[1], (D, D), dtype=jnp.float32) * s, 'bq': jnp.zeros((D,), dtype=jnp.float32), 'Wk': jax.random.normal(ks[2], (D, D), dtype=jnp.float32) * s, 'bk': jnp.zeros((D,), dtype=jnp.float32), 'Wv': jax.random.normal(ks[3], (D, D), dtype=jnp.float32) * s, 'bv': jnp.zeros((D,), dtype=jnp.float32), 'Wo': jax.random.normal(ks[4], (D, D), dtype=jnp.float32) * s, 'bo': jnp.zeros((D,), dtype=jnp.float32)}
    _L0_attn_in = _L0_attn_setup()

    def _L0_ffn_setup():
        import jax, jax.numpy as jnp
        import numpy as np
        GOLDEN_CENTER = 1.0 / np.e
        GOLDEN_LOWER = 0.5 - np.log(4.0 / 3.0)
        GOLDEN_UPPER = 0.5

        def _golden_weights(x, Wr, temperature):
            inh = jax.nn.sigmoid(x @ Wr / temperature)
            in_zone = (inh >= GOLDEN_LOWER) & (inh <= GOLDEN_UPPER)
            distance = jnp.abs(inh - GOLDEN_CENTER)
            weights = jnp.exp(-distance / 0.1) * in_zone.astype(x.dtype)
            wsum = jnp.sum(weights, axis=-1, keepdims=True)
            no_expert = wsum < 1e-08
            fb = jnp.exp(-distance / 0.3)
            _, top2 = jax.lax.top_k(fb, 2)
            fb_mask = jnp.sum(jax.nn.one_hot(top2, weights.shape[-1], dtype=x.dtype), axis=-2)
            fb_w = fb * fb_mask
            fb_w = fb_w / jnp.maximum(jnp.sum(fb_w, axis=-1, keepdims=True), 1e-08)
            weights = jnp.where(no_expert, fb_w, weights)
            weights = weights / jnp.maximum(jnp.sum(weights, axis=-1, keepdims=True), 1e-08)
            return weights
        key = jax.random.key(seed)
        ks = jax.random.split(key, 5)
        B, T, D, E, F = (2, 256, 256, 8, 256)
        s_in = 1.0 / np.sqrt(D)
        s_f = 1.0 / np.sqrt(F)
        return {'x': jax.random.normal(ks[0], (B, T, D), dtype=jnp.float32), 'Wg': jax.random.normal(ks[1], (E, D, F), dtype=jnp.float32) * s_in, 'Wu': jax.random.normal(ks[2], (E, D, F), dtype=jnp.float32) * s_in, 'Wd': jax.random.normal(ks[3], (E, F, D), dtype=jnp.float32) * s_f, 'Wr': jax.random.normal(ks[4], (D, E), dtype=jnp.float32) * s_in, 'temperature': jnp.ones((1,), dtype=jnp.float32)}
    _L0_ffn_in = _L0_ffn_setup()
    _d = {'L0_attn_x': _L0_attn_in['x'], 'L0_attn_Wq': _L0_attn_in['Wq'], 'L0_attn_bq': _L0_attn_in['bq'], 'L0_attn_Wk': _L0_attn_in['Wk'], 'L0_attn_bk': _L0_attn_in['bk'], 'L0_attn_Wv': _L0_attn_in['Wv'], 'L0_attn_bv': _L0_attn_in['bv'], 'L0_attn_Wo': _L0_attn_in['Wo'], 'L0_attn_bo': _L0_attn_in['bo'], 'L0_ffn_Wg': _L0_ffn_in['Wg'], 'L0_ffn_Wu': _L0_ffn_in['Wu'], 'L0_ffn_Wd': _L0_ffn_in['Wd'], 'L0_ffn_Wr': _L0_ffn_in['Wr'], 'L0_ffn_temperature': _L0_ffn_in['temperature']}
    _x0 = _d['L0_attn_x']
    _d['L0_attn_x'] = jax.random.normal(jax.random.fold_in(jax.random.key(seed), 1), (4, 512, 256), dtype=_x0.dtype)
    del _x0
    return _d

def reference(L0_attn_x, L0_attn_Wq, L0_attn_bq, L0_attn_Wk, L0_attn_bk, L0_attn_Wv, L0_attn_bv, L0_attn_Wo, L0_attn_bo, L0_ffn_Wg, L0_ffn_Wu, L0_ffn_Wd, L0_ffn_Wr, L0_ffn_temperature):

    def _L0_attn_ref(x, Wq, bq, Wk, bk, Wv, bv, Wo, bo):
        import jax, jax.numpy as jnp
        import numpy as np
        B, T, D = (4, 256, 256)
        H = 16
        HD = D // H
        b, t, _ = x.shape

        def split_heads(y):
            return y.reshape(b, t, H, HD).transpose(0, 2, 1, 3)
        q = split_heads(x @ Wq.T + bq)
        k = split_heads(x @ Wk.T + bk)
        v = split_heads(x @ Wv.T + bv)
        scale = 1.0 / jnp.sqrt(jnp.float32(HD))
        scores = jnp.einsum('bhqd,bhkd->bhqk', q, k) * scale
        causal = jnp.triu(jnp.ones((t, t), dtype=bool), k=1)
        scores = jnp.where(causal, -jnp.inf, scores)
        attn = jax.nn.softmax(scores, axis=-1)
        ctx = jnp.einsum('bhqk,bhkd->bhqd', attn, v)
        ctx = ctx.transpose(0, 2, 1, 3).reshape(b, t, D)
        return ctx @ Wo.T + bo

    def _L0_ffn_ref(x, Wg, Wu, Wd, Wr, temperature):
        import jax, jax.numpy as jnp
        import numpy as np
        GOLDEN_CENTER = 1.0 / np.e
        GOLDEN_LOWER = 0.5 - np.log(4.0 / 3.0)
        GOLDEN_UPPER = 0.5

        def _golden_weights(x, Wr, temperature):
            inh = jax.nn.sigmoid(x @ Wr / temperature)
            in_zone = (inh >= GOLDEN_LOWER) & (inh <= GOLDEN_UPPER)
            distance = jnp.abs(inh - GOLDEN_CENTER)
            weights = jnp.exp(-distance / 0.1) * in_zone.astype(x.dtype)
            wsum = jnp.sum(weights, axis=-1, keepdims=True)
            no_expert = wsum < 1e-08
            fb = jnp.exp(-distance / 0.3)
            _, top2 = jax.lax.top_k(fb, 2)
            fb_mask = jnp.sum(jax.nn.one_hot(top2, weights.shape[-1], dtype=x.dtype), axis=-2)
            fb_w = fb * fb_mask
            fb_w = fb_w / jnp.maximum(jnp.sum(fb_w, axis=-1, keepdims=True), 1e-08)
            weights = jnp.where(no_expert, fb_w, weights)
            weights = weights / jnp.maximum(jnp.sum(weights, axis=-1, keepdims=True), 1e-08)
            return weights
        weights = _golden_weights(x, Wr, temperature)
        gate = jnp.einsum('btd,edf->betf', x, Wg)
        up = jnp.einsum('btd,edf->betf', x, Wu)
        h = jax.nn.silu(gate) * up
        e_out = jnp.einsum('betf,efd->betd', h, Wd)
        out = jnp.einsum('bte,betd->btd', weights, e_out)
        return out
    x = L0_attn_x
    x = x + 0.5 * _L0_ffn_ref(_layernorm(x, axis=-1), L0_ffn_Wg, L0_ffn_Wu, L0_ffn_Wd, L0_ffn_Wr, L0_ffn_temperature)
    x = x + _L0_attn_ref(_layernorm(x, axis=-1), L0_attn_Wq, L0_attn_bq, L0_attn_Wk, L0_attn_bk, L0_attn_Wv, L0_attn_bv, L0_attn_Wo, L0_attn_bo)
    x = x + 0.5 * _L0_ffn_ref(_layernorm(x, axis=-1), L0_ffn_Wg, L0_ffn_Wu, L0_ffn_Wd, L0_ffn_Wr, L0_ffn_temperature)
    return x

_drawn_inputs = setup_inputs


def setup_inputs(seed=0):
    import zlib

    import numpy as np

    out = dict(_drawn_inputs(seed))
    spreads = {'L0_attn_bq': (0.0, 0.8),
     'L0_attn_bk': (0.0, 0.8),
     'L0_attn_bv': (0.0, 0.1),
     'L0_attn_bo': (0.0, 0.1)}
    factors = {'L0_attn_Wq': 8.0, 'L0_attn_Wk': 8.0, 'L0_attn_Wv': 3.303}
    for name, (base, spread) in spreads.items():
        noise = np.random.default_rng([zlib.crc32(name.encode()), seed]).standard_normal(out[name].shape)
        drawn = base * np.exp(spread * noise) if base else spread * noise
        out[name] = jnp.asarray(drawn.astype(out[name].dtype))
    for name, factor in factors.items():
        out[name] = (out[name] * factor).astype(out[name].dtype)
    return out
```

```python
import concourse.bass as bass
from concourse import mybir
from contextlib import ExitStack

F32 = mybir.dt.float32
F32R = mybir.dt.float32r
BF16 = mybir.dt.bfloat16
I32 = mybir.dt.int32
ALU = mybir.AluOpType
ACT = mybir.ActivationFunctionType
AX = mybir.AxisListType

P = 128
BATCH, T, D = 4, 512, 256
E, F = 8, 256
H = 16
HD = D // H
KT = D // P
FT = F // P
NT = BATCH * T // P
QT = T // P
EPS = 1e-5
GOLD = 0.36787944117144233
LOWER = 0.21231792754821915
UPPER = 0.5
MASKED = -1.0e30
RSQRT_SEED = float(0x5F3759DF)


class Chain:

    def __init__(self, eng, sem):
        self.eng, self.sem, self.count = eng, sem, 0

    def __call__(self, ins):
        self.count += 1
        ins.then_inc(self.sem, 1)
        self.eng.wait_ge(self.sem, self.count)


def settle(eng, passed):
    eng.sem_inc(passed, 1)


def f32(ap):
    return ap.bitcast(F32)


def emit_rstd(nc, chain, stats, mv, var, rstd, tmp):
    for t in range(NT):
        ins = nc.vector.bn_aggr(mv[:, t, :], stats[:, t, :])
        if t == NT - 1:
            chain(ins)
    chain(nc.vector.tensor_scalar(var[:], mv[:, :, 1], EPS, None, ALU.add))
    chain(nc.vector.tensor_scalar(rstd[:].bitcast(I32), var[:].bitcast(I32), -0.5, RSQRT_SEED,
                                  ALU.mult, ALU.add))
    for _ in range(4):
        chain(nc.vector.tensor_tensor(tmp[:], rstd[:], rstd[:], ALU.mult))
        chain(nc.vector.tensor_tensor(tmp[:], tmp[:], var[:], ALU.mult))
        chain(nc.vector.tensor_scalar(tmp[:], tmp[:], -0.5, 1.5, ALU.mult, ALU.add))
        chain(nc.vector.tensor_tensor(rstd[:], rstd[:], tmp[:], ALU.mult))


def load_phase(nc, A, R):
    with ExitStack() as ctx:
        def sb(name, shape, dt=F32):
            return ctx.enter_context(nc.sbuf_tensor(name, shape, dt))

        def sem(name):
            return ctx.enter_context(nc.semaphore(name))

        NSTAGE = 3
        stage_gu = [sb(f"stage_gu{i}", [P, KT, 2 * F]) for i in range(NSTAGE)]
        stage_d = [sb(f"stage_d{i}", [P, FT, D]) for i in range(NSTAGE)]
        stage_a = sb("stage_a", [P, 4, KT, D])
        stage_r = sb("stage_r", [P, KT, E])
        x_in = [sem(f"x_in{b}") for b in range(BATCH)]
        small_in = sem("small_in")
        expert_in = [sem(f"expert_in{i}") for i in range(NSTAGE)]
        attn_in = sem("attn_in")
        hi_done, lo_done = sem("ld_hi_done"), sem("ld_lo_done")
        consts = sem("consts")
        own = sem("ld_own")

        wq_t = [A[n].rearrange("(k p) o -> p k o", p=P) for n in ("WqT", "WkT", "WvT", "WoT")]

        with nc.Block() as block:
            @block.sync
            def _(sp):
                for b in range(BATCH):
                    sp.dma_start(R["x"][:, b * QT:(b + 1) * QT, :],
                                 A["x"][b].rearrange("(q p) d -> p q d", p=P)).then_inc(x_in[b], 16)
                for e in range(E):
                    i = e % NSTAGE
                    if e >= NSTAGE:
                        sp.wait_ge(lo_done, 2 * (e - NSTAGE + 1))
                    sp.dma_start(stage_gu[i][:, :, 0:F],
                                 A["Wg"][e].rearrange("(k p) f -> p k f", p=P)).then_inc(expert_in[i], 16)
                    sp.dma_start(stage_gu[i][:, :, F:2 * F],
                                 A["Wu"][e].rearrange("(k p) f -> p k f", p=P)).then_inc(expert_in[i], 16)
                    sp.dma_start(stage_d[i][:, :, :],
                                 A["Wd"][e].rearrange("(k p) d -> p k d", p=P)).then_inc(expert_in[i], 16)
                for w in range(4):
                    sp.dma_start(stage_a[:, w, :, :], wq_t[w]).then_inc(attn_in, 16)

            @block.scalar
            def _(act):
                act.dma_start(stage_r[:, :, :], A["Wr"].rearrange("(k p) e -> p k e", p=P)).then_inc(small_in, 16)
                act.dma_start(R["temp"][:, :], A["temp"]).then_inc(small_in, 16)
                act.dma_start(R["bq"][:, :], A["bq"]).then_inc(small_in, 16)
                act.dma_start(R["bk"][:, :], A["bk"]).then_inc(small_in, 16)
                act.dma_start(R["bv"][:, :], A["bv"]).then_inc(small_in, 16)
                act.dma_start(R["bo"][:, :], A["bo"]).then_inc(small_in, 16)
                for e in range(E):
                    i = e % NSTAGE
                    act.wait_ge(expert_in[i], 48 * (e // NSTAGE + 1))
                    nc.scalar.activation(R["wgu_hi"][:, e, :, :], stage_gu[i][:, :, :], ACT.Copy).then_inc(hi_done, 1)
                    nc.scalar.activation(R["wd"][:, e, :, 0:D], stage_d[i][:, :, :], ACT.Copy).then_inc(hi_done, 1)
                act.wait_ge(attn_in, 64)
                nc.scalar.activation(R["wa"][:, :, :, 0:D].rearrange("p w k d -> p (w k) d"),
                                     stage_a[:, :, :, :].rearrange("p w k d -> p (w k) d"), ACT.Copy).then_inc(hi_done, 1)
                act.wait_ge(small_in, 96)
                nc.scalar.activation(R["wr"][:, :, 0:E], stage_r[:, :, :], ACT.Copy).then_inc(hi_done, 1)

            @block.vector
            def _(dve):
                chain = Chain(dve, own)
                for b in range(BATCH):
                    dve.wait_ge(x_in[b], 16)
                    for q in range(QT):
                        ins = nc.vector.bn_stats(R["stats"][:, b * QT + q, :], R["x"][:, b * QT + q, :])
                chain(ins)
                emit_rstd(nc, chain, R["stats"], R["mv"], R["var"], R["rstd"], R["ntmp"])
                for e in range(E):
                    i = e % NSTAGE
                    dve.wait_ge(hi_done, 2 * e + 1)
                    nc.vector.tensor_tensor(R["wgu_lo"][:, e, :, :], stage_gu[i][:, :, :],
                                            f32(R["wgu_hi"][:, e, :, :]), ALU.subtract).then_inc(lo_done, 1)
                    dve.wait_ge(hi_done, 2 * e + 2)
                    nc.vector.tensor_tensor(R["wd"][:, e, :, D:2 * D], stage_d[i][:, :, :],
                                            f32(R["wd"][:, e, :, 0:D]), ALU.subtract).then_inc(lo_done, 1)
                dve.wait_ge(hi_done, 2 * E + 1)
                nc.vector.tensor_tensor(R["wa"][:, :, :, D:2 * D].rearrange("p w k d -> p (w k) d"),
                                        stage_a[:, :, :, :].rearrange("p w k d -> p (w k) d"),
                                        f32(R["wa"][:, :, :, 0:D]).rearrange("p w k d -> p (w k) d"),
                                        ALU.subtract).then_inc(lo_done, 1)
                dve.wait_ge(hi_done, 2 * E + 2)
                nc.vector.tensor_tensor(R["wr"][:, :, E:2 * E], stage_r[:, :, :],
                                        f32(R["wr"][:, :, 0:E]), ALU.subtract).then_inc(lo_done, 1)
                chain(nc.vector.reciprocal(R["half_rt"][:, :], R["temp"][:, :]))
                chain(nc.vector.tensor_scalar(R["half_rt"][:, :], R["half_rt"][:, :], 0.5, None, ALU.mult))

            @block.gpsimd
            def _(pool):
                chain = Chain(pool, consts)
                chain(nc.gpsimd.memset(R["ident"][:, :], 0.0))
                chain(nc.gpsimd.affine_select(out=R["ident"][:, :], in_=R["ident"][:, :], compare_op=ALU.not_equal,
                                              fill=1.0, base=0, pattern=[[-1, P]], channel_multiplier=1))
                chain(nc.gpsimd.iota(R["expert_no"][:, :], pattern=[[1, E]], base=0, channel_multiplier=0,
                                     allow_small_or_imprecise_dtypes=True))


def ffn_phase(nc, R, out, tag, entry_rstd):
    with ExitStack() as ctx:
        def sb(name, shape, dt=F32):
            return ctx.enter_context(nc.sbuf_tensor(f"{tag}_{name}", shape, dt))

        def sem(name):
            return ctx.enter_context(nc.semaphore(f"{tag}_{name}"))

        def bank(name):
            return ctx.enter_context(nc.psum_tensor(f"{tag}_{name}", [P, 512], F32))

        gu_ps = [bank(f"gu_ps{i}") for i in range(2)]
        ht_ps = [bank(f"ht_ps{i}") for i in range(2)]
        out_ps = [bank(f"out_ps{i}") for i in range(2)]
        xt_ps = bank("xt_ps")

        xn = sb("xn", [P, D])
        xt_hi = [sb(f"xt_hi{i}", [P, KT, P], F32R) for i in range(2)]
        xt_lo = [sb(f"xt_lo{i}", [P, KT, P], F32R) for i in range(2)]
        silu = [sb(f"silu{i}", [P, F]) for i in range(2)]
        hid = [sb(f"hid{i}", [P, F]) for i in range(2)]
        ht_hi = [sb(f"ht_hi{i}", [P, FT, P], F32R) for i in range(2)]
        ht_lo = [sb(f"ht_lo{i}", [P, FT, P], F32R) for i in range(2)]
        acc = sb("acc", [P, D])
        wts = [sb(f"wts{i}", [P, E]) for i in range(2)]
        z = sb("z", [P, E])
        th = sb("th", [P, E])
        inh = sb("inh", [P, E])
        zone = sb("zone", [P, E])
        ndist = sb("ndist", [P, E])
        texp = sb("texp", [P, 2, E])
        rnum = sb("rnum", [P, 2, E])
        rden = sb("rden", [P, 2, E])
        top8 = sb("top8", [P, 8])
        topi = sb("topi", [P, 8], mybir.dt.uint32)
        topf = sb("topf", [P, 8])
        pick = sb("pick", [P, E])
        wz = sb("wz", [P, E])
        sums = sb("sums", [P, 8])

        gu_done = sem("gu_done")
        gu_free = sem("gu_free")
        silu_done = sem("silu_done")
        tr_done = sem("tr_done")
        hi_done = sem("hi_done")
        lo_done = sem("lo_done")
        down_done = sem("down_done")
        out_free = sem("out_free")
        ln_done = sem("ln_done")
        xtr_done = sem("xtr_done")
        xhi_done = sem("xhi_done")
        xlo_done = sem("xlo_done")
        rmm_done = sem("rmm_done")
        rz_done = sem("rz_done")
        th_done = sem("th_done")
        nd_done = sem("nd_done")
        te_done = sem("te_done")
        own = sem("own")
        hid_own = sem("hid_own")
        x_done = sem("x_done")
        out_sem = sem("out_sem")
        passed = sem("passed")

        ROUTE_OPS = 19
        PAIRS = NT // 2
        STEPS = 2 * E

        def weave(step_main, step_pre, eng):
            with eng.Fori(0, PAIRS - 1) as p:
                for k in range(STEPS):
                    step_main(p * 2, k, 2)
                    step_pre(p * 2 + k // E + 1, (k // E + 1) % 2, k % E)
            last = (PAIRS - 1) * 2
            for k in range(STEPS):
                step_main(last, k, STEPS - 1 - k)
                if k // E == 0:
                    step_pre(NT - 1, 1, k % E)

        with nc.Block() as block:
            @block.tensor
            def _(pe):
                mm = nc.tensor.matmul

                def gate_up(t0, k):
                    n = t0 * E + k
                    i, e = (k // E) % 2, k % E
                    if e == 0:
                        pe.wait_ge(xlo_done, (t0 + k // E) + 1)
                    pe.wait_ge(gu_free, n + 1)
                    o = gu_ps[k % 2][:, :]
                    for c in range(KT):
                        mm(o, xt_hi[i][:, c, :], R["wgu_hi"][:, e, c, :], start=c == 0, stop=False)
                        mm(o, xt_hi[i][:, c, :], R["wgu_lo"][:, e, c, :], start=False, stop=False)
                        last = mm(o, xt_lo[i][:, c, :], R["wgu_hi"][:, e, c, :], start=False, stop=c == KT - 1)
                    last.then_inc(gu_done, 1)

                def transpose_hidden(t0, k):
                    n = t0 * E + k
                    pe.wait_ge(gu_free, n + 3)
                    for c in range(FT):
                        last = nc.tensor.transpose(ht_ps[k % 2][:, c * P:(c + 1) * P],
                                                   hid[k % 2][:, c * P:(c + 1) * P], R["ident"][:, :])
                    last.then_inc(tr_done, 1)

                def down(t0, k):
                    n = t0 * E + k
                    i, e = (k // E) % 2, k % E
                    pe.wait_ge(lo_done, n + 1)
                    if e == 0:
                        pe.wait_ge(out_free, (t0 + k // E) + 1)
                    o, w = out_ps[i], R["wd"]
                    mm(o[:, :], ht_hi[k % 2][:, 0, :], w[:, e, 0, :], start=e == 0, stop=False)
                    mm(o[:, 0:D], ht_lo[k % 2][:, 0, :], w[:, e, 0, 0:D], start=False, stop=False)
                    mm(o[:, 0:D], ht_lo[k % 2][:, 1, :], w[:, e, 1, 0:D], start=False, stop=False)
                    mm(o[:, :], ht_hi[k % 2][:, 1, :], w[:, e, 1, :], start=False,
                       stop=e == E - 1).then_inc(down_done, 1)

                def main(t0, k, ahead):
                    if ahead >= 2:
                        gate_up(t0, k + 2)
                    if ahead >= 1:
                        transpose_hidden(t0, k + 1)
                    down(t0, k)

                def transpose_x(t, i):
                    pe.wait_ge(ln_done, t + 1)
                    for c in range(KT):
                        last = nc.tensor.transpose(xt_ps[:, c * P:(c + 1) * P], xn[:, c * P:(c + 1) * P],
                                                   R["ident"][:, :])
                    last.then_inc(xtr_done, 1)

                def router(t, i):
                    pe.wait_ge(xlo_done, t + 1)
                    o = xt_ps[:, D:D + 2 * E]
                    for c in range(KT):
                        mm(o, xt_hi[i][:, c, :], R["wr"][:, c, :], start=c == 0, stop=False)
                        last = mm(o, xt_lo[i][:, c, :], R["wr"][:, c, :], start=False, stop=c == KT - 1)
                    last.then_inc(rmm_done, 1)

                def pre(t, i, e):
                    if e == 1:
                        pe.wait_ge(rz_done, t)
                        transpose_x(t, i)
                    if e == 2:
                        router(t, i)

                transpose_x(0, 0)
                router(0, 0)
                gate_up(0, 0)
                gate_up(0, 1)
                transpose_hidden(0, 0)
                weave(main, pre, pe)

            @block.scalar
            def _(act):
                act.sem_inc(down_done, 2)

                def make_silu(t0, k):
                    n = t0 * E + k
                    act.wait_ge(gu_done, n + 1)
                    nc.scalar.activation(silu[k % 2][:, :], gu_ps[k % 2][:, 0:F], ACT.Silu).then_inc(silu_done, 1)

                def hidden_hi(t0, k):
                    n = t0 * E + k
                    act.wait_ge(tr_done, n + 1)
                    act.wait_ge(down_done, n + 1)
                    nc.scalar.activation(ht_hi[k % 2][:, :, :].rearrange("p c t -> p (c t)"),
                                         ht_ps[k % 2][:, 0:F], ACT.Copy).then_inc(hi_done, 1)

                def main(t0, k, ahead):
                    if ahead >= 2:
                        make_silu(t0, k + 2)
                    if ahead >= 1:
                        hidden_hi(t0, k + 1)

                def x_hi(t, i):
                    act.wait_ge(xtr_done, t + 1)
                    nc.scalar.activation(xt_hi[i][:, :, :].rearrange("p c t -> p (c t)"),
                                         xt_ps[:, 0:D], ACT.Copy).then_inc(xhi_done, 1)

                def tanh_sigmoid(t):
                    act.wait_ge(rz_done, t + 1)
                    nc.scalar.activation(th[:, :], z[:, :], ACT.Tanh, scale=R["half_rt"][:, 0:1]).then_inc(th_done, 1)

                def tanh_exp(t):
                    act.wait_ge(nd_done, t + 1)
                    nc.scalar.activation(texp[:, 0, :], ndist[:, :], ACT.Tanh, scale=5.0)
                    nc.scalar.activation(texp[:, 1, :], ndist[:, :], ACT.Tanh, scale=1.0 / 0.6).then_inc(te_done, 1)

                def pre(t, i, e):
                    if e == 1:
                        x_hi(t, i)
                    if e == 3:
                        tanh_sigmoid(t)
                    if e == 4:
                        tanh_exp(t)

                x_hi(0, 0)
                tanh_sigmoid(0)
                tanh_exp(0)
                make_silu(0, 0)
                make_silu(0, 1)
                hidden_hi(0, 0)
                weave(main, pre, act)

            @block.vector
            def _(dve):
                start = Chain(dve, ctx.enter_context(nc.semaphore(f"{tag}_start")))
                if entry_rstd:
                    emit_rstd(nc, start, R["stats"], R["mv"], R["var"], R["rstd"], R["ntmp"])
                dve.sem_inc(gu_free, 2)
                dve.sem_inc(out_free, 2)

                def make_hidden(t0, k):
                    n = t0 * E + k
                    i, e = (k // E) % 2, k % E
                    if e == 0:
                        dve.wait_ge(hid_own, (t0 + k // E) + 1)
                    dve.wait_ge(silu_done, n + 1)
                    nc.vector.scalar_tensor_tensor(out=hid[k % 2][:, :], in0=silu[k % 2][:, :],
                                                   scalar=wts[i][:, e:e + 1], in1=gu_ps[k % 2][:, F:2 * F],
                                                   op0=ALU.mult, op1=ALU.mult).then_inc(gu_free, 1)

                def hidden_lo(t0, k):
                    n = t0 * E + k
                    dve.wait_ge(hi_done, n + 1)
                    nc.vector.tensor_tensor(ht_lo[k % 2][:, :, :].rearrange("p c t -> p (c t)"),
                                            ht_ps[k % 2][:, 0:F],
                                            f32(ht_hi[k % 2][:, :, :]).rearrange("p c t -> p (c t)"),
                                            ALU.subtract).then_inc(lo_done, 1)

                def add_tile(t, i):
                    dve.wait_ge(down_done, (t + 1) * E + 2)
                    xt = R["x"][:, t, :]
                    nc.vector.tensor_tensor(acc[:, :], out_ps[i][:, 0:D], xt, ALU.add).then_inc(x_done, 1)
                    dve.wait_ge(x_done, t + 1)
                    nc.vector.tensor_tensor(xt, out_ps[i][:, D:2 * D], acc[:, :], ALU.add).then_inc(out_free, 1)
                    if out is None:
                        dve.wait_ge(out_free, t + 3)
                        nc.vector.bn_stats(R["stats"][:, t, :], xt)

                def main(t0, k, ahead):
                    if ahead >= 2:
                        make_hidden(t0, k + 2)
                    if ahead >= 1:
                        hidden_lo(t0, k + 1)
                    if k % E == E - 1:
                        add_tile((t0 + k // E), k // E)

                def layernorm(t):
                    nc.vector.tensor_scalar(xn[:, :], R["x"][:, t, :], R["mv"][:, t, 0:1], R["rstd"][:, bass.ds(t, 1)],
                                            ALU.subtract, ALU.mult).then_inc(ln_done, 1)

                def x_lo(t, i):
                    dve.wait_ge(xhi_done, t + 1)
                    nc.vector.tensor_tensor(xt_lo[i][:, :, :].rearrange("p c t -> p (c t)"), xt_ps[:, 0:D],
                                            f32(xt_hi[i][:, :, :]).rearrange("p c t -> p (c t)"),
                                            ALU.subtract).then_inc(xlo_done, 1)

                def read_router(t):
                    dve.wait_ge(rmm_done, t + 1)
                    nc.vector.tensor_reduce(out=z[:, :],
                                            in_=xt_ps[:, D:D + 2 * E].rearrange("p (s e) -> p e s", s=2),
                                            axis=AX.X, op=ALU.add).then_inc(rz_done, 1)

                class Link:
                    count = 0

                def link(t, ins):
                    Link.count += 1
                    ins.then_inc(own, 1)
                    dve.wait_ge(own, t * ROUTE_OPS + Link.count)

                def distances(t):
                    Link.count = 0
                    dve.wait_ge(th_done, t + 1)
                    link(t, nc.vector.tensor_scalar(inh[:, :], th[:, :], 0.5, 0.5, ALU.mult, ALU.add))
                    link(t, nc.vector.tensor_scalar(zone[:, :], inh[:, :], UPPER, None, ALU.is_le))
                    link(t, nc.vector.scalar_tensor_tensor(out=zone[:, :], in0=inh[:, :], scalar=LOWER,
                                                           in1=zone[:, :], op0=ALU.is_ge, op1=ALU.mult))
                    link(t, nc.vector.tensor_scalar(inh[:, :], inh[:, :], GOLD, None, ALU.subtract))
                    nc.vector.scalar_tensor_tensor(out=ndist[:, :], in0=inh[:, :], scalar=-1.0, in1=inh[:, :],
                                                   op0=ALU.mult, op1=ALU.min).then_inc(nd_done, 1)
                    dve.wait_ge(nd_done, t + 1)
                    settle(dve, passed)
                    link(t, nc.vector.max(top8[:, :], ndist[:, :]))
                    settle(dve, passed)
                    link(t, nc.vector.max_index(topi[:, :], top8[:, :], ndist[:, :]))
                    link(t, nc.vector.tensor_copy(topf[:, :], topi[:, :]))
                    link(t, nc.vector.tensor_scalar(pick[:, :], R["expert_no"][:, :], topf[:, 0:1], None,
                                                    ALU.is_equal))
                    link(t, nc.vector.scalar_tensor_tensor(out=pick[:, :], in0=R["expert_no"][:, :],
                                                           scalar=topf[:, 1:2], in1=pick[:, :],
                                                           op0=ALU.is_equal, op1=ALU.add))

                def routing(t, i):
                    dve.wait_ge(te_done, t + 1)
                    nc.vector.tensor_scalar(rnum[:, :, :], texp[:, :, :], 1.0, None, ALU.add)
                    link(t, nc.vector.tensor_scalar(rden[:, :, :], texp[:, :, :], -1.0, 1.0, ALU.mult, ALU.add))
                    link(t, nc.vector.reciprocal(rden[:, :, :], rden[:, :, :]))
                    link(t, nc.vector.tensor_tensor(rnum[:, :, :], rnum[:, :, :], rden[:, :, :], ALU.mult))
                    nc.vector.scalar_tensor_tensor(out=wz[:, :], in0=rnum[:, 0, :], scalar=1.0, in1=zone[:, :],
                                                   op0=ALU.mult, op1=ALU.mult, accum_out=sums[:, 0:1])
                    link(t, nc.vector.scalar_tensor_tensor(out=pick[:, :], in0=rnum[:, 1, :], scalar=1.0,
                                                           in1=pick[:, :], op0=ALU.mult, op1=ALU.mult,
                                                           accum_out=sums[:, 1:2]))
                    link(t, nc.vector.tensor_scalar(sums[:, 1:2], sums[:, 1:2], 1e-8, None, ALU.max))
                    link(t, nc.vector.reciprocal(sums[:, 2:3], sums[:, 1:2]))
                    link(t, nc.vector.scalar_tensor_tensor(out=sums[:, 3:4], in0=sums[:, 0:1], scalar=1e-8,
                                                           in1=sums[:, 2:3], op0=ALU.is_lt, op1=ALU.mult))
                    link(t, nc.vector.scalar_tensor_tensor(out=wz[:, :], in0=pick[:, :], scalar=sums[:, 3:4],
                                                           in1=wz[:, :], op0=ALU.mult, op1=ALU.add,
                                                           accum_out=sums[:, 4:5]))
                    link(t, nc.vector.tensor_scalar(sums[:, 4:5], sums[:, 4:5], 1e-8, None, ALU.max))
                    link(t, nc.vector.reciprocal(sums[:, 5:6], sums[:, 4:5]))
                    nc.vector.tensor_scalar(wts[i][:, :], wz[:, :], sums[:, 5:6], 0.5,
                                            ALU.mult, ALU.mult).then_inc(hid_own, 1)
                    assert Link.count == ROUTE_OPS

                def pre(t, i, e):
                    if e == 0:
                        layernorm(t)
                    if e == 1:
                        x_lo(t, i)
                    if e == 2:
                        read_router(t)
                    if e == 3:
                        distances(t)
                    if e == 4:
                        routing(t, i)

                layernorm(0)
                x_lo(0, 0)
                read_router(0)
                distances(0)
                routing(0, 0)
                make_hidden(0, 0)
                make_hidden(0, 1)
                hidden_lo(0, 0)
                weave(main, pre, dve)

            if out is not None:
                @block.sync
                def _(sp):
                    with sp.Fori(0, NT) as t:
                        sp.wait_ge(out_free, t + 3)
                        settle(sp, passed)
                        sp.dma_start(out[bass.ds(t * P, P), :], R["x"][:, t, :]).then_inc(out_sem, 16)
                    sp.wait_ge(out_sem, 16 * NT)


def attn_phase(nc, R, qk_dram, v_dram):
    with ExitStack() as ctx:
        def sb(name, shape, dt=F32):
            return ctx.enter_context(nc.sbuf_tensor(f"at_{name}", shape, dt))

        def sem(name):
            return ctx.enter_context(nc.semaphore(f"at_{name}"))

        def bank(name):
            return ctx.enter_context(nc.psum_tensor(f"at_{name}", [P, 512], F32))

        Q_PARTS = (0, 0, 0, 1, 1, 2)
        K_PARTS = (0, 1, 2, 0, 1, 0)
        NBLK = len(Q_PARTS)
        KROWS = NBLK * HD
        SROWS = KROWS + 2
        GH = 4
        NG = H // GH
        HM = P // HD
        HT = T // 2

        NA, NB = 4, 2
        ra = [bank(f"ra{i}") for i in range(NA)]
        rb = [bank(f"rb{i}") for i in range(NB)]
        ctx_ps = bank("ctx_ps")
        mt_ps = bank("mt_ps")

        xn = sb("xn", [P, D])
        x2_hi = sb("x2_hi", [P, KT, HT], F32R)
        x2_lo = sb("x2_lo", [P, KT, HT], F32R)
        parts = [sb(f"parts{i}", [P, 3, HT], BF16) for i in range(2)]
        rest = sb("rest", [P, HT])
        q_st = sb("q_st", [P, H, T], BF16)
        k_st = sb("k_st", [P, H, T], BF16)
        v_out = sb("v_out", [P, D])
        vg = [sb(f"vg{i}", [P, QT, GH, 2 * HD]) for i in range(2)]
        probs = sb("probs", [P, 2, 5, T])
        v_half = sb("v_half", [P, D])
        work = sb("work", [P, D])
        junk = sb("junk", [P, NA, T], BF16)
        mask = sb("mask", [P, T], BF16)
        mx = [sb(f"mx{i}", [P, P]) for i in range(2)]
        mp = sb("mp", [GH * QT, 2, P], BF16)
        cx = sb("cx", [P, T])
        rec = sb("rec", [P, QT * GH])
        cn = sb("cn", [P, QT, D])
        ct_hi = sb("ct_hi", [P, KT, P], F32R)
        ct_lo = sb("ct_lo", [P, KT, P], F32R)

        ra_full = sem("ra_full")
        ra_free = sem("ra_free")
        rb_full = sem("rb_full")
        rb_free = sem("rb_free")
        ln_done = sem("ln_done")
        xhi_done = sem("xhi_done")
        qk_h = sem("qk_h")
        qk_m = sem("qk_m")
        qk_l = sem("qk_l")
        v_own = sem("v_own")
        t1_own = sem("t1_own")
        qk_st = [sem(f"qk_st{i}") for i in range(2)]
        v_st = sem("v_st")
        st_ld = [sem(f"st_ld{m}") for m in range(KT)]
        v_ld = [sem(f"v_ld{i}") for i in range(2)]
        mt_full = sem("mt_full")
        mh_done = sem("mh_done")
        ml_done = sem("ml_done")
        mx_ld = [sem(f"mx_ld{g}") for g in range(NG)]
        mk_done = sem("mk_done")
        pv_done = sem("pv_done")
        cx_done = sem("cx_done")
        chi_done = sem("chi_done")
        wo_own = sem("wo_own")
        consts = sem("consts")
        passed = sem("passed")
        passed_pool, passed_sp = sem("passed_pool"), sem("passed_sp")

        LAYOUT = [[(0, 0, 0)], [(1, 0, 0)], [(0, 1, 0), (0, 3, 384)], [(1, 1, 0), (1, 3, 384)],
                  [(0, 2, 0), (1, 2, 256)]]
        WHERE = {(h, j): (k, c) for k, row in enumerate(LAYOUT) for h, j, c in row}
        PAIR_BANKS = len(LAYOUT)
        GB = 2 * PAIR_BANKS
        NS = NG * GB
        MASKS = 3

        def half(f):
            x = [("ln", 2 * f), ("x", 2 * f), ("ln", 2 * f + 1), ("x", 2 * f + 1)]
            qk = [(kind, 4 * f + u) for u in range(4) for kind in ("qk", "qkl")]
            return x, qk, [("v", 2 * f), ("v", 2 * f + 1)]

        x_a, qk_a, v_a = half(0)
        x_b, qk_b, v_b = half(1)
        PIECES = [x_a + qk_a[0:6], qk_a[6:8] + v_a + x_b + qk_b[0:4], qk_b[4:8] + v_b, []]
        AHEAD = 7

        def slot(g, more):
            nxt = [("max", g + 1, s) for s in range(GH * QT)] if g + 1 < NG or more else []
            pieces = list(PIECES[g]) if more else []
            items = [("mt", g)] + nxt[0:2] + ([("t1", g - 1)] if g else []) + nxt[2:AHEAD]
            nxt = nxt[AHEAD:]
            for r in range(GB):
                items.append(("exp", g, r))
                items += nxt[0:1]
                nxt = nxt[1:]
                n = -(-len(pieces) // (GB - r))
                items += pieces[0:n]
                pieces = pieces[n:]
            return items + [("pv", g)]

        TAIL = [("t1", NG - 1), ("t2", 0), ("wo", 0), ("t2", 1), ("wo", 1), ("t2", 2), ("wo", 2),
                ("t2", 3), ("wo", 3)]
        FIRST = x_a + qk_a + v_a + x_b + qk_b + v_b + [("max", 0, s) for s in range(GH * QT)]
        BODY = [it for g in range(NG) for it in slot(g, True)] + TAIL
        LAST = [it for g in range(NG) for it in slot(g, False)] + TAIL
        USERS = ("x", "qk", "v", "max", "t1", "t2", "wo")

        def uses(items):
            return [it for it in items if it[0] in USERS]

        N0, N1 = len(uses(FIRST)), len(uses(BODY))
        assert N0 % NA == 0 and N1 % NA == 0

        class Place:

            def __init__(self, items, base, b, nb):
                self.base, self.b, self.nb = base, b, nb
                self.at = {it: j for j, it in enumerate(uses(items))}

            def bank(self, it):
                return ra[self.at[it] % NA]

            def full(self, it):
                return self.base + self.at[it] + 1

            def left(self, it):
                return self.base + self.at[it] + 1 + NA

            def batch(self, it):
                if it[0] in ("ln", "x", "qk", "qkl", "v"):
                    return self.nb
                return self.nb if it[0] == "max" and it[1] % NG == 0 else self.b

        def run(eng, do):
            for it in FIRST:
                do(Place(FIRST, 0, 0, 0), it)
            with eng.Fori(0, BATCH - 1) as b:
                for it in BODY:
                    do(Place(BODY, b * N1 + N0, b, b + 1), it)
            for it in LAST:
                do(Place(LAST, (BATCH - 1) * N1 + N0, BATCH - 1, None), it)

        with nc.Block() as block:
            @block.tensor
            def _(pe):
                mm = nc.tensor.matmul

                def transpose(out, in_):
                    return nc.tensor.transpose(out, in_, R["ident"][:, :])

                def do(pl, it):
                    kind, b = it[0], pl.batch(it)
                    if kind in USERS:
                        o = pl.bank(it)
                        pe.wait_ge(ra_free, pl.base + pl.at[it] + 1)
                    if kind == "x":
                        i = it[1]
                        pe.wait_ge(ln_done, b * QT + i + 1)
                        for c in range(KT):
                            last = transpose(o[:, c * P:(c + 1) * P], xn[:, c * P:(c + 1) * P])
                        last.then_inc(ra_full, 1)
                    if kind == "qk":
                        f, m, w = it[1] // 4, it[1] % 4 // 2, it[1] % 2
                        if it[1] % 4 == 0:
                            pe.wait_ge(ra_free, pl.left(("x", 2 * f + 1)))
                        for c in range(KT):
                            w_hi = R["wa"][:, w, c, m * P:(m + 1) * P]
                            w_lo = R["wa"][:, w, c, D + m * P:D + (m + 1) * P]
                            mm(o[:, 0:HT], w_hi, x2_hi[:, c, :], start=c == 0, stop=False)
                            mm(o[:, 0:HT], w_hi, x2_lo[:, c, :], start=False, stop=False)
                            last = mm(o[:, 0:HT], w_lo, x2_hi[:, c, :], start=False, stop=c == KT - 1)
                        last.then_inc(ra_full, 1)
                    if kind == "v":
                        tok = slice(it[1] % 2 * P, (it[1] % 2 + 1) * P)
                        mm(o[:, :], x2_hi[:, 0, tok], R["wa"][:, 2, 0, :], start=True, stop=False)
                        mm(o[:, 0:D], x2_lo[:, 0, tok], R["wa"][:, 2, 0, 0:D], start=False, stop=False)
                        mm(o[:, 0:D], x2_lo[:, 1, tok], R["wa"][:, 2, 1, 0:D], start=False, stop=False)
                        mm(o[:, :], x2_hi[:, 1, tok], R["wa"][:, 2, 1, :], start=False,
                           stop=True).then_inc(ra_full, 1)
                    if kind == "max":
                        g, hh, i = it[1] % NG, it[2] // QT, it[2] % QT
                        h = g * GH + hh
                        if it[2] == 0 and g % 2 == 0:
                            pe.wait_ge(st_ld[g // 2], 32 * NBLK * (b + 1))
                        mm(o[:, 0:(i + 1) * P], q_st[0:KROWS, h, i * P:(i + 1) * P],
                           k_st[0:KROWS, h, 0:(i + 1) * P], start=True, stop=True).then_inc(ra_full, 1)
                    if kind == "mt":
                        g = it[1]
                        pe.wait_ge(ml_done, b * NG + g + 1)
                        pe.wait_ge(ra_free, pl.left(("max", g, GH * QT - 1)) if g else pl.base + NA)
                        transpose(mt_ps[:, 0:P], mx[g % 2][:, :]).then_inc(mt_full, 1)
                    if kind == "exp":
                        g, r = it[1], it[2]
                        pr, k = r // PAIR_BANKS, r % PAIR_BANKS
                        at = g * GB + r
                        if r == 0:
                            pe.wait_ge(mx_ld[g], 32 * (b + 1))
                        pe.wait_ge(rb_free, b * NS + at + 1)
                        for hp, j, c in LAYOUT[k]:
                            h = g * GH + 2 * pr + hp
                            last = mm(rb[at % NB][:, c:c + T - j * P], k_st[0:SROWS, h, j * P:(j + 1) * P],
                                      q_st[0:SROWS, h, j * P:T], start=True, stop=True)
                        last.then_inc(rb_full, 1)
                    if kind == "pv":
                        g = it[1]
                        pe.wait_ge(mk_done, MASKS * 2 * (b * NG + g + 1))
                        pe.wait_ge(v_ld[g % 2], 16 * QT * (b * 2 + g // 2 + 1))
                        pe.wait_ge(cx_done, b * NG + g + 1)
                        for j in range(QT):
                            for hh in range(GH):
                                k, c = WHERE[(hh % 2, j)]
                                last = mm(ctx_ps[32 * hh:32 * hh + 32, j * P:T], vg[g % 2][:, j, hh, :],
                                          probs[:, hh // 2, k, c:c + T - j * P], start=j == 0,
                                          stop=j == QT - 1)
                        last.then_inc(pv_done, 1)
                    if kind == "t1":
                        pe.wait_ge(cx_done, b * NG + it[1] + 2)
                        for i in range(QT):
                            last = transpose(o[:, i * P:(i + 1) * P], cx[:, i * P:(i + 1) * P])
                        last.then_inc(ra_full, 1)
                    if kind == "t2":
                        if it[1] == 0:
                            pe.wait_ge(ra_free, pl.left(("t1", NG - 1)))
                        for c in range(KT):
                            last = transpose(o[:, c * P:(c + 1) * P], cn[:, it[1], c * P:(c + 1) * P])
                        last.then_inc(ra_full, 1)
                    if kind == "wo":
                        pe.wait_ge(ra_free, pl.left(("t2", it[1])))
                        mm(o[:, :], ct_hi[:, 0, :], R["wa"][:, 3, 0, :], start=True, stop=False)
                        mm(o[:, 0:D], ct_lo[:, 0, :], R["wa"][:, 3, 0, 0:D], start=False, stop=False)
                        mm(o[:, 0:D], ct_lo[:, 1, :], R["wa"][:, 3, 1, 0:D], start=False, stop=False)
                        mm(o[:, :], ct_hi[:, 1, :], R["wa"][:, 3, 1, :], start=False,
                           stop=True).then_inc(ra_full, 1)

                pe.sem_inc(pv_done, 1)
                pe.wait_ge(consts, 7)
                run(pe, do)

            @block.scalar
            def _(act):
                act.sem_inc(rb_free, NB)
                act.sem_inc(cx_done, 1)

                def do(pl, it):
                    kind, b = it[0], pl.batch(it)
                    if kind == "x":
                        part = slice(it[1] % 2 * P, (it[1] % 2 + 1) * P)
                        act.wait_ge(ra_full, pl.full(it))
                        nc.scalar.activation(x2_hi[:, :, part],
                                             pl.bank(it)[:, 0:D].rearrange("p (c t) -> p c t", c=KT),
                                             ACT.Copy).then_inc(xhi_done, 1)
                    if kind == "qk":
                        m, bias = it[1] % 4 // 2, R["bq"] if it[1] % 2 == 0 else R["bk"]
                        act.wait_ge(ra_full, pl.full(it))
                        if it[1] > 1 or pl.b is not pl.nb:
                            act.wait_ge(qk_st[it[1] % 2], 16 * (b * 4 + it[1] // 2))
                        nc.scalar.activation(parts[it[1] % 2][:, 0, :], pl.bank(it)[:, 0:HT], ACT.Identity,
                                             bias=bias[:, m:m + 1]).then_inc(qk_h, 1)
                    if kind == "qkl":
                        act.wait_ge(ra_free, pl.left(("qk", it[1])))
                        nc.scalar.activation(parts[it[1] % 2][:, 1, :], rest[:, :], ACT.Copy).then_inc(qk_m, 1)
                    if kind == "mt":
                        g = it[1]
                        act.wait_ge(mt_full, b * NG + g + 1)
                        nc.scalar.activation(mp[:, 0, :], mt_ps[0:GH * QT, 0:P], ACT.Copy).then_inc(mh_done, 1)
                        act.wait_ge(ml_done, b * NG + g + 2)
                        for c in range(2):
                            row = KROWS + c
                            act.dma_start(q_st[row:row + 1, g * GH:(g + 1) * GH, :].rearrange("a h t -> a (h t)"),
                                          mp[:, c, :]).then_inc(mx_ld[g], 16)
                    if kind == "exp":
                        g, r = it[1], it[2]
                        at = g * GB + r
                        if r == 0:
                            act.wait_ge(pv_done, b * NG + g + 1)
                        act.wait_ge(rb_full, b * NS + at + 1)
                        nc.scalar.activation(probs[:, r // PAIR_BANKS, r % PAIR_BANKS, :], rb[at % NB][:, :],
                                             ACT.Exp, scale=HD ** -0.5).then_inc(rb_free, 1)
                    if kind == "pv":
                        act.wait_ge(pv_done, b * NG + it[1] + 2)
                        nc.scalar.activation(cx[:, :], ctx_ps[:, :], ACT.Copy).then_inc(cx_done, 1)
                    if kind == "t2":
                        act.wait_ge(ra_full, pl.full(it))
                        nc.scalar.activation(ct_hi[:, :, :].rearrange("p c t -> p (c t)"), pl.bank(it)[:, 0:D],
                                             ACT.Copy).then_inc(chi_done, 1)

                run(act, do)

            @block.gpsimd
            def _(pool):
                chain = Chain(pool, consts)
                chain(nc.gpsimd.memset(mask[:, :], 0.0))
                chain(nc.gpsimd.affine_select(out=mask[:, T - P:T], in_=mask[:, T - P:T], compare_op=ALU.is_ge,
                                              fill=MASKED, base=0, pattern=[[-1, P]], channel_multiplier=1))
                for i in range(2):
                    chain(nc.gpsimd.memset(vg[i][:, :, :, HD:2 * HD], 1.0))
                chain(nc.gpsimd.memset(k_st[KROWS:SROWS, :, :], -1.0))
                for i in range(2):
                    chain(nc.gpsimd.memset(mx[i][:, :], 0.0))

                def keep_causal(view, n):
                    nc.gpsimd.affine_select(out=view, in_=view, compare_op=ALU.is_ge, fill=0.0, base=0,
                                            pattern=[[0, n], [1, P]], channel_multiplier=-1).then_inc(mk_done, 1)

                with pool.Fori(0, BATCH) as b:
                    for g in range(NG):
                        for pr in range(2):
                            pool.wait_ge(rb_free, b * NS + (2 * g + pr + 1) * PAIR_BANKS + NB)
                            settle(pool, passed_pool)
                            keep_causal(probs[:, pr, :, 0:P], 5)
                            keep_causal(probs[:, pr, 2:4, 3 * P:4 * P], 2)
                            keep_causal(probs[:, pr, 4:5, 2 * P:3 * P], 1)

            @block.sync
            def _(sp):
                def load_stacks(b, m):
                    for i in range(2):
                        sp.wait_ge(qk_st[i], 16 * (b * 4 + 3 + m))
                    settle(sp, passed_sp)
                    for w, (stack, order) in enumerate(((q_st, Q_PARTS), (k_st, K_PARTS))):
                        for j, part in enumerate(order):
                            src = qk_dram[b, 2 * m + w, part].rearrange("(h f) t -> f h t", f=HD)
                            sp.dma_start(stack[j * HD:(j + 1) * HD, m * HM:(m + 1) * HM, :],
                                         src).then_inc(st_ld[m], 16)

                def load_v(b, g):
                    for j in range(QT):
                        sp.dma_start(vg[g % 2][:, j, :, 0:HD],
                                     v_dram[b, j, :, g * GH * HD:(g + 1) * GH * HD]
                                     .rearrange("p (h f) -> p h f", f=HD)).then_inc(v_ld[g % 2], 16)

                def do(pl, it):
                    kind, b = it[0], pl.batch(it)
                    if kind == "mt" and it[1] < NG - 1:
                        sp.wait_ge(pv_done, b * NG + it[1] + 1)
                        settle(sp, passed_sp)
                        load_v(b, it[1] + 1)
                    if kind == "mt" and it[1] == NG - 1 and pl.nb is not None:
                        sp.wait_ge(pv_done, b * NG + it[1] + 1)
                        sp.wait_ge(v_st, 16 * QT * (pl.nb + 1))
                        settle(sp, passed_sp)
                        load_v(pl.nb, 0)
                    if kind == "qkl":
                        f, u = it[1] // 4, it[1] % 4
                        sp.wait_ge(qk_l, b * 8 + it[1] + 1)
                        settle(sp, passed_sp)
                        sp.dma_start(qk_dram[b, u, :, :, f * HT:(f + 1) * HT].rearrange("c p t -> p c t"),
                                     parts[it[1] % 2][:, :, :]).then_inc(qk_st[it[1] % 2], 16)
                    if kind == "v":
                        sp.wait_ge(ra_free, pl.left(it))
                        settle(sp, passed_sp)
                        sp.dma_start(v_dram[b, it[1]], v_out[:, :]).then_inc(v_st, 16)
                    if kind == "pv" and it[1] % 2 == 1 and pl.nb is not None:
                        m = it[1] // 2
                        sp.wait_ge(rb_full, b * NS + (it[1] + 1) * GB)
                        settle(sp, passed_sp)
                        load_stacks(pl.nb, m)
                    if it == FIRST[-1] and pl.b is pl.nb:
                        load_stacks(0, 0)
                        load_stacks(0, 1)
                        sp.wait_ge(v_st, 16 * QT)
                        settle(sp, passed_sp)
                        load_v(0, 0)

                run(sp, do)

            @block.vector
            def _(dve):
                start = Chain(dve, ctx.enter_context(nc.semaphore("at_start")))
                emit_rstd(nc, start, R["stats"], R["mv"], R["var"], R["rstd"], R["ntmp"])
                dve.sem_inc(ra_free, NA)
                dve.sem_inc(ml_done, 1)
                dve.wait_ge(consts, 7)

                def do(pl, it):
                    kind, b = it[0], pl.batch(it)
                    if kind in USERS and kind not in ("x", "qk", "t2"):
                        dve.wait_ge(ra_full, pl.full(it))
                    if kind in USERS:
                        o = pl.bank(it)

                    if kind == "ln":
                        t = b * QT + it[1]
                        nc.vector.tensor_scalar(xn[:, :], R["x"][:, t, :], R["mv"][:, t, 0:1],
                                                R["rstd"][:, bass.ds(t, 1)], ALU.subtract,
                                                ALU.mult).then_inc(ln_done, 1)
                    if kind == "x":
                        part = slice(it[1] % 2 * P, (it[1] % 2 + 1) * P)
                        dve.wait_ge(xhi_done, b * QT + it[1] + 1)
                        nc.vector.tensor_tensor(x2_lo[:, :, part], o[:, 0:D].rearrange("p (c t) -> p c t", c=KT),
                                                f32(x2_hi[:, :, part]), ALU.subtract).then_inc(ra_free, 1)
                    if kind == "qk":
                        m, bias = it[1] % 4 // 2, R["bq"] if it[1] % 2 == 0 else R["bk"]
                        dve.wait_ge(qk_h, b * 8 + it[1] + 1)
                        if it[1] > 0 or pl.b is not pl.nb:
                            dve.wait_ge(qk_l, b * 8 + it[1])
                        nc.vector.scalar_tensor_tensor(out=rest[:, :], in0=o[:, 0:HT], scalar=bias[:, m:m + 1],
                                                       in1=parts[it[1] % 2][:, 0, :], op0=ALU.add,
                                                       op1=ALU.subtract).then_inc(ra_free, 1)
                    if kind == "qkl":
                        dve.wait_ge(qk_m, b * 8 + it[1] + 1)
                        nc.vector.tensor_tensor(parts[it[1] % 2][:, 2, :], rest[:, :], parts[it[1] % 2][:, 1, :],
                                                ALU.subtract).then_inc(qk_l, 1)
                    if kind == "v":
                        n = b * QT + it[1]
                        dve.wait_ge(ra_free, pl.left(it) - 1)
                        nc.vector.tensor_tensor(v_half[:, :], o[:, 0:D], R["bv"][:, :], ALU.add).then_inc(v_own, 1)
                        dve.wait_ge(v_own, n + 1)
                        if it[1] > 0 or pl.b is not pl.nb:
                            dve.wait_ge(v_st, 16 * n)
                        nc.vector.tensor_tensor(v_out[:, :], o[:, D:2 * D], v_half[:, :], ALU.add).then_inc(ra_free, 1)
                    if kind == "max":
                        s, w = it[2], (it[2] % QT + 1) * P
                        settle(dve, passed)
                        nc.vector.tensor_tensor_reduce(out=junk[:, pl.at[it] % NA, 0:w], in0=o[:, 0:w], in1=mask[:, T - w:T],
                                                       scale=1.0, scalar=-3.0e38, op0=ALU.add, op1=ALU.max,
                                                       accum_out=mx[it[1] % 2][:, s:s + 1]).then_inc(ra_free, 1)
                    if kind == "mt":
                        dve.wait_ge(mh_done, b * NG + it[1] + 1)
                        nc.vector.tensor_tensor(mp[:, 1, :], mt_ps[0:GH * QT, 0:P], mp[:, 0, :],
                                                ALU.subtract).then_inc(ml_done, 1)
                    if kind == "t1":
                        g = it[1]
                        heads = o[:, :].rearrange("p (n c) -> p n c", c=2 * HD)
                        dve.wait_ge(ra_free, pl.left(it) - 1)
                        nc.vector.reciprocal(rec[:, :], heads[:, :, HD]).then_inc(t1_own, 1)
                        dve.wait_ge(t1_own, b * NG + g + 1)
                        nc.vector.tensor_tensor(
                            cn[:, :, g * GH * HD:(g + 1) * GH * HD].rearrange("p i (h f) -> p i h f", f=HD),
                            o[:, :].rearrange("p (i h c) -> p i h c", i=QT, c=2 * HD)[:, :, :, 0:HD],
                            rec[:, :].rearrange("p (i h) -> p i h", i=QT).unsqueeze(3).to_broadcast([P, QT, GH, HD]),
                            ALU.mult).then_inc(ra_free, 1)
                    if kind == "t2":
                        dve.wait_ge(chi_done, b * QT + it[1] + 1)
                        nc.vector.tensor_tensor(ct_lo[:, :, :].rearrange("p c t -> p (c t)"), o[:, 0:D],
                                                f32(ct_hi[:, :, :]).rearrange("p c t -> p (c t)"),
                                                ALU.subtract).then_inc(ra_free, 1)
                    if kind == "wo":
                        t = b * QT + it[1]
                        xt = R["x"][:, t, :]
                        dve.wait_ge(ra_free, pl.left(it) - 1)
                        nc.vector.tensor_tensor(work[:, :], o[:, 0:D], xt, ALU.add).then_inc(wo_own, 1)
                        dve.wait_ge(wo_own, 2 * t + 1)
                        nc.vector.tensor_tensor(work[:, :], work[:, :], R["bo"][:, :], ALU.add).then_inc(wo_own, 1)
                        dve.wait_ge(wo_own, 2 * t + 2)
                        nc.vector.tensor_tensor(xt, o[:, D:2 * D], work[:, :], ALU.add).then_inc(ra_free, 1)
                        dve.wait_ge(ra_free, pl.left(it))
                        nc.vector.bn_stats(R["stats"][:, t, :], xt)

                run(dve, do)


def build(nc, A, out):
    with ExitStack() as ctx:
        def sb(name, shape, dt=F32):
            return ctx.enter_context(nc.sbuf_tensor(name, shape, dt))

        R = {
            "x": sb("x_res", [P, NT, D]),
            "wgu_hi": sb("wgu_hi", [P, E, KT, 2 * F], F32R),
            "wgu_lo": sb("wgu_lo", [P, E, KT, 2 * F], F32R),
            "wd": sb("wd", [P, E, FT, 2 * D], F32R),
            "wa": sb("wa", [P, 4, KT, 2 * D], F32R),
            "wr": sb("wr", [P, KT, 2 * E], F32R),
            "temp": sb("temp", [P, 1]),
            "half_rt": sb("half_rt", [P, 1]),
            "bq": sb("bq", [P, KT]),
            "bk": sb("bk", [P, KT]),
            "bv": sb("bv", [P, D]),
            "bo": sb("bo", [P, D]),
            "ident": sb("ident", [P, P]),
            "expert_no": sb("expert_no", [P, E]),
            "stats": sb("stats", [P, NT, 6]),
            "mv": sb("mv", [P, NT, 2]),
            "var": sb("var", [P, NT]),
            "rstd": sb("rstd", [P, NT]),
            "ntmp": sb("ntmp", [P, NT]),
        }
        qk_dram = nc.dram_tensor("qk_parts", (BATCH, 2 * KT, 3, P, T), BF16, kind="Internal").ap()
        v_dram = nc.dram_tensor("v_rows", (BATCH, QT, P, D), F32, kind="Internal").ap()
        load_phase(nc, A, R)
        ffn_phase(nc, R, None, "f1", entry_rstd=False)
        attn_phase(nc, R, qk_dram, v_dram)
        ffn_phase(nc, R, out, "f2", entry_rstd=True)


def kernel(**inputs):
    import numpy as np
    import concourse.bacc as bacc
    from concourse.bass_utils import run_bass_kernel_spmd

    def raw(name):
        return np.asarray(inputs["L0_" + name])

    def row(name):
        return np.ascontiguousarray(np.broadcast_to(raw(name)[None, :], (P, raw(name).shape[0])))

    arrays = {
        "x": np.ascontiguousarray(raw("attn_x")),
        "Wg": np.ascontiguousarray(raw("ffn_Wg")),
        "Wu": np.ascontiguousarray(raw("ffn_Wu")),
        "Wd": np.ascontiguousarray(raw("ffn_Wd")),
        "Wr": np.ascontiguousarray(raw("ffn_Wr")),
        "temp": row("ffn_temperature"),
        "WqT": np.ascontiguousarray(raw("attn_Wq").T),
        "WkT": np.ascontiguousarray(raw("attn_Wk").T),
        "WvT": np.ascontiguousarray(raw("attn_Wv").T),
        "WoT": np.ascontiguousarray(raw("attn_Wo").T),
        "bq": np.ascontiguousarray(raw("attn_bq").reshape(KT, P).T),
        "bk": np.ascontiguousarray(raw("attn_bk").reshape(KT, P).T),
        "bv": row("attn_bv"),
        "bo": row("attn_bo"),
    }
    nc = bacc.Bacc("TRN2", target_bir_lowering=False, num_devices=1, dynamic_dma_scratch_size=1024)
    A = {n: nc.dram_tensor("in_" + n, a.shape, mybir.dt.from_np(a.dtype), kind="ExternalInput").ap()
         for n, a in arrays.items()}
    out = nc.dram_tensor("out_x", (BATCH * T, D), F32, kind="ExternalOutput").ap()
    build(nc, A, out)
    r = run_bass_kernel_spmd(nc, [{"in_" + n: a for n, a in arrays.items()}], core_ids=[0])
    return np.asarray(r.results[0]["out_x"]).reshape(BATCH, T, D)
```
